# Optimizing a Trainium2 kernel written in Bass

```python
import numpy as np
import jax
import jax.numpy as jnp

def _softmax(x, axis=-1):
    return jax.nn.softmax(x, axis=axis)

def _gelu(x):
    return jax.nn.gelu(x, approximate=True)

def _silu(x):
    return jax.nn.silu(x)

def _sigmoid(x):
    return jax.nn.sigmoid(x)

def _layernorm(x, axis=-1, eps=1e-05):
    m = jnp.mean(x, axis=axis, keepdims=True)
    v = jnp.var(x, axis=axis, keepdims=True)
    return (x - m) / jnp.sqrt(v + eps)

def _scatter_add(tgt, idx, src, axis=0):
    return tgt.at[idx].add(src)

def _segment_sum(src, seg, n):
    return jax.ops.segment_sum(src, seg, n)
kernel_name = 'mk_dlrm_tower_d1_rec_r8_c0bde5'

def setup_inputs(seed: int=0):
    np.random.seed(seed)
    _w = jnp.asarray

    def _rec_inputs():
        import jax
        import jax.numpy as jnp
        _tk = jax.random.key(seed)
        dense_ctx = jax.random.normal(jax.random.fold_in(_tk, 190), (512, 16), jnp.float32)
        ids = jnp.stack([jax.random.randint(jax.random.fold_in(_tk, 200 + f), (512,), 0, v, jnp.int32) for f, v in enumerate([1000, 1000, 1250, 1000, 12500, 1000, 12500, 1250])], axis=1)
        tbl_0 = 0.05 * jax.random.normal(jax.random.fold_in(_tk, 500 + 0), (1000, 1024), jnp.float32)
        tbl_1 = 0.05 * jax.random.normal(jax.random.fold_in(_tk, 500 + 1), (1000, 1024), jnp.float32)
        tbl_2 = 0.05 * jax.random.normal(jax.random.fold_in(_tk, 500 + 2), (1250, 1024), jnp.float32)
        tbl_3 = 0.05 * jax.random.normal(jax.random.fold_in(_tk, 500 + 3), (1000, 1024), jnp.float32)
        tbl_4 = 0.05 * jax.random.normal(jax.random.fold_in(_tk, 500 + 4), (12500, 1024), jnp.float32)
        tbl_5 = 0.05 * jax.random.normal(jax.random.fold_in(_tk, 500 + 5), (1000, 1024), jnp.float32)
        tbl_6 = 0.05 * jax.random.normal(jax.random.fold_in(_tk, 500 + 6), (12500, 1024), jnp.float32)
        tbl_7 = 0.05 * jax.random.normal(jax.random.fold_in(_tk, 500 + 7), (1250, 1024), jnp.float32)
        _rk = jax.random.fold_in(_tk, 7)
        W_top1 = 0.0310087 * jax.random.normal(jax.random.fold_in(_tk, 801), (1040, 512), jnp.float32)
        W_top2 = 0.0441942 * jax.random.normal(jax.random.fold_in(_tk, 802), (512, 256), jnp.float32)
        W_top3 = 0.0625 * jax.random.normal(jax.random.fold_in(_tk, 803), (256, 1), jnp.float32)
        b_top1 = jnp.zeros((512,), jnp.float32)
        b_top2 = jnp.zeros((256,), jnp.float32)
        return (dense_ctx, ids, tbl_0, tbl_1, tbl_2, tbl_3, tbl_4, tbl_5, tbl_6, tbl_7, W_top1, b_top1, W_top2, b_top2, W_top3)
    dense_ctx, ids, tbl_0, tbl_1, tbl_2, tbl_3, tbl_4, tbl_5, tbl_6, tbl_7, W_top1, b_top1, W_top2, b_top2, W_top3 = _rec_inputs()

    def _L0_rec_setup():
        import jax, jax.numpy as jnp
        import numpy as np
        B, F, H = (1024, 8, 1024)

        def _linear_params(key, fan_in, fan_out):
            kw, kb = jax.random.split(key)
            w = jax.random.normal(kw, (fan_in, fan_out), dtype=jnp.float32) * 0.02
            b = jax.random.normal(kb, (fan_out,), dtype=jnp.float32) * 0.02
            return (w, b)
        key = jax.random.key(seed)
        ks = jax.random.split(key, 7)
        field_vectors = jax.random.normal(ks[0], (B, F, H), dtype=jnp.float32)
        Wn1, bn1 = _linear_params(ks[1], H, H)
        Wn2, bn2 = _linear_params(ks[2], H, H)
        Wa1, ba1 = _linear_params(ks[3], 2 * H, H)
        Wa2, ba2 = _linear_params(ks[4], H, H)
        Wo1, bo1 = _linear_params(ks[5], 2 * H, H)
        Wo2, bo2 = _linear_params(ks[6], H, H)
        not_idx = jnp.array([2, 3], dtype=jnp.int64)
        and_pairs = jnp.array([[0, 1], [2, 3]], dtype=jnp.int64)
        or_pairs = jnp.array([[4, 5]], dtype=jnp.int64)
        return {'field_vectors': field_vectors, 'Wn1': Wn1, 'bn1': bn1, 'Wn2': Wn2, 'bn2': bn2, 'Wa1': Wa1, 'ba1': ba1, 'Wa2': Wa2, 'ba2': ba2, 'Wo1': Wo1, 'bo1': bo1, 'Wo2': Wo2, 'bo2': bo2, 'not_idx': not_idx, 'and_pairs': and_pairs, 'or_pairs': or_pairs}
    _L0_rec_all = _L0_rec_setup()
    _L0_rec_in = {k: v for k, v in _L0_rec_all.items() if k in ('Wn1', 'bn1', 'Wn2', 'bn2', 'Wa1', 'ba1', 'Wa2', 'ba2', 'Wo1', 'bo1', 'Wo2', 'bo2', 'not_idx', 'and_pairs', 'or_pairs')}
    del _L0_rec_all
    return {'dense_ctx': dense_ctx, 'ids': ids, 'tbl_0': tbl_0, 'tbl_1': tbl_1, 'tbl_2': tbl_2, 'tbl_3': tbl_3, 'tbl_4': tbl_4, 'tbl_5': tbl_5, 'tbl_6': tbl_6, 'tbl_7': tbl_7, 'W_top1': W_top1, 'b_top1': b_top1, 'W_top2': W_top2, 'b_top2': b_top2, 'W_top3': W_top3, 'L0_rec_Wn1': _L0_rec_in['Wn1'], 'L0_rec_bn1': _L0_rec_in['bn1'], 'L0_rec_Wn2': _L0_rec_in['Wn2'], 'L0_rec_bn2': _L0_rec_in['bn2'], 'L0_rec_Wa1': _L0_rec_in['Wa1'], 'L0_rec_ba1': _L0_rec_in['ba1'], 'L0_rec_Wa2': _L0_rec_in['Wa2'], 'L0_rec_ba2': _L0_rec_in['ba2'], 'L0_rec_Wo1': _L0_rec_in['Wo1'], 'L0_rec_bo1': _L0_rec_in['bo1'], 'L0_rec_Wo2': _L0_rec_in['Wo2'], 'L0_rec_bo2': _L0_rec_in['bo2'], 'L0_rec_not_idx': _L0_rec_in['not_idx'], 'L0_rec_and_pairs': _L0_rec_in['and_pairs'], 'L0_rec_or_pairs': _L0_rec_in['or_pairs']}

def reference(dense_ctx, ids, tbl_0, tbl_1, tbl_2, tbl_3, tbl_4, tbl_5, tbl_6, tbl_7, W_top1, b_top1, W_top2, b_top2, W_top3, L0_rec_Wn1, L0_rec_bn1, L0_rec_Wn2, L0_rec_bn2, L0_rec_Wa1, L0_rec_ba1, L0_rec_Wa2, L0_rec_ba2, L0_rec_Wo1, L0_rec_bo1, L0_rec_Wo2, L0_rec_bo2, L0_rec_not_idx, L0_rec_and_pairs, L0_rec_or_pairs):
    import jax
    import jax.numpy as jnp

    def _L0_rec_ref(field_vectors, Wn1, bn1, Wn2, bn2, Wa1, ba1, Wa2, ba2, Wo1, bo1, Wo2, bo2, not_idx, and_pairs, or_pairs):
        import jax, jax.numpy as jnp
        import numpy as np
        B, F, H = (1024, 8, 1024)

        def _linear_params(key, fan_in, fan_out):
            kw, kb = jax.random.split(key)
            w = jax.random.normal(kw, (fan_in, fan_out), dtype=jnp.float32) * 0.02
            b = jax.random.normal(kb, (fan_out,), dtype=jnp.float32) * 0.02
            return (w, b)
        num_fields = field_vectors.shape[1]
        x_not = jnp.take(field_vectors, not_idx, axis=1)
        t = jnp.tanh(jax.nn.relu(x_not @ Wn1 + bn1) @ Wn2 + bn2)
        iv = field_vectors.at[:, not_idx, :].set(t)

        def pair_fuse(pairs, W1, b1, W2, b2):
            v = jnp.concatenate([jnp.take(iv, pairs[:, 0], axis=1), jnp.take(iv, pairs[:, 1], axis=1)], axis=-1)
            return jax.nn.relu(v @ W1 + b1) @ W2 + b2
        and_out = pair_fuse(and_pairs, Wa1, ba1, Wa2, ba2)
        or_out = pair_fuse(or_pairs, Wo1, bo1, Wo2, bo2)
        processed = jnp.zeros((num_fields,), dtype=field_vectors.dtype).at[and_pairs.reshape(-1)].set(1.0).at[or_pairs.reshape(-1)].set(1.0)
        remaining = 1.0 - processed
        sum_res = and_out.sum(axis=1) + or_out.sum(axis=1) + jnp.einsum('bfh,f->bh', iv, remaining)
        count = and_pairs.shape[0] + or_pairs.shape[0] + remaining.sum()
        return sum_res / count
    e = jnp.stack([tbl_0[ids[:, 0]], tbl_1[ids[:, 1]], tbl_2[ids[:, 2]], tbl_3[ids[:, 3]], tbl_4[ids[:, 4]], tbl_5[ids[:, 5]], tbl_6[ids[:, 6]], tbl_7[ids[:, 7]]], axis=1)
    z = _L0_rec_ref(e, L0_rec_Wn1, L0_rec_bn1, L0_rec_Wn2, L0_rec_bn2, L0_rec_Wa1, L0_rec_ba1, L0_rec_Wa2, L0_rec_ba2, L0_rec_Wo1, L0_rec_bo1, L0_rec_Wo2, L0_rec_bo2, L0_rec_not_idx, L0_rec_and_pairs, L0_rec_or_pairs)
    z = z.reshape(z.shape[0], -1)
    h = jnp.concatenate([z, dense_ctx], axis=1)
    h = jnp.maximum(h @ W_top1 + b_top1, 0.0)
    h = jnp.maximum(h @ W_top2 + b_top2, 0.0)
    y = h @ W_top3
    return y

_drawn_inputs = setup_inputs


def setup_inputs(seed=0):
    import zlib

    import numpy as np

    out = dict(_drawn_inputs(seed))
    spreads = {'b_top1': (0.0, 0.1), 'b_top2': (0.0, 0.1)}
    factors = {'tbl_0': 4.372,
     'tbl_1': 4.602,
     'tbl_2': 8.0,
     'tbl_3': 8.0,
     'tbl_4': 4.307,
     'tbl_5': 4.536,
     'L0_rec_Wn1': 8.0,
     'L0_rec_bn1': 8.0,
     'L0_rec_Wn2': 8.0,
     'L0_rec_bn2': 8.0,
     'L0_rec_Wa1': 2.995,
     'L0_rec_ba1': 3.97,
     'L0_rec_Wo1': 3.459,
     'L0_rec_bo1': 8.0,
     'L0_rec_Wo2': 2.676}
    for name, (base, spread) in spreads.items():
        noise = np.random.default_rng([zlib.crc32(name.encode()), seed]).standard_normal(out[name].shape)
        drawn = base * np.exp(spread * noise) if base else spread * noise
        out[name] = jnp.asarray(drawn.astype(out[name].dtype))
    for name, factor in factors.items():
        out[name] = (out[name] * factor).astype(out[name].dtype)
    return out
```

```python
from contextlib import ExitStack

import numpy as np
import concourse.bass as bass
from concourse import mybir

F32 = mybir.dt.float32
F32R = mybir.dt.float32r
I32 = mybir.dt.int32
U32 = mybir.dt.uint32
ALU = mybir.AluOpType
ACT = mybir.ActivationFunctionType
AX = mybir.AxisListType

P = 128
B = 512
H = 1024
FIELDS = 8
VOCAB = (1000, 1000, 1250, 1000, 12500, 1000, 12500, 1250)
ROWS = sum(VOCAB)
BT = B // P
KT = H // P
QUARTERS = 4
QW = H // QUARTERS
DENSE = 16
DENSE_ROWS = 64 + DENSE
TOP1, TOP2 = 512, 256
PICKED = 8
PAIR_ELEMENTS = 6
BIG = float(1 << 20)

CHUNK = 1024
WARM = 16
NOT1, NOT2, AND_A, AND_B, OR, SUM, TOPA, TOPB, CHUNKS = 0, 8, 16, 32, 48, 64, 80, 84, 85
AND_AGAIN = AND_B - AND_A

G_NOT1, G_NOT2, G_AND_A, G_AND_B, G_OR, G_SUM, G_TOPA, G_TOPB = 0, 16, 32, 40, 48, 56, 64, 68

T_NOT, T_AND_A, T_AND_B, T_OR, T_REST = 0, 16, 32, 48, 64

C_BN1, C_BN2, C_BA1, C_BA2, C_BO1, C_BO2, C_BT1, C_BT2, C_W3, PARAMS = 0, 8, 16, 24, 32, 40, 48, 52, 54, 56

K_VOC, K_LAST, K_BASE, K_IOTA, K_QUARTER, K_TILE, K_STAGE, CONSTS = 0, 8, 16, 24, 32, 36, 84, 132
HEAD_IDS = BT * FIELDS
HEAD = HEAD_IDS + PICKED + CONSTS


def constants():
    row = np.zeros(CONSTS, np.int32)
    row[K_VOC:K_VOC + 8] = VOCAB
    row[K_LAST:K_LAST + 8] = np.array(VOCAB) - 1
    row[K_BASE:K_BASE + 8] = np.cumsum((0,) + VOCAB[:-1])
    row[K_IOTA:K_IOTA + 8] = np.arange(8)
    row[K_QUARTER:K_QUARTER + 4] = np.arange(4)
    row[K_TILE:K_TILE + 48] = np.tile(np.arange(8), 6)
    row[K_STAGE:K_STAGE + 48] = [16 + (e if e < 2 else k % 2) for e in range(6) for k in range(8)]
    return row


def build(nc, head, params, tables, weights, dense_t, w_dense, out):
    with ExitStack() as ctx:
        def sb(name, shape, dt=F32):
            return ctx.enter_context(nc.sbuf_tensor(name, shape, dt))

        def sem(name):
            return ctx.enter_context(nc.semaphore(name))

        x = sb("x", [P, 2, 2, KT, B], F32R)
        hid = sb("hid", [P, 2, 2, KT, B], F32R)
        nt = sb("nt", [P, 18, B])
        rows = sb("rows", [P, BT, H])
        w_raw = sb("w_raw", [P, 2, CHUNK])
        w_hi = sb("w_hi", [P, 2, CHUNK], F32R)
        w_lo = sb("w_lo", [P, 2, CHUNK], F32R)
        ident = sb("ident", [P, P])
        par = sb("par", [P, PARAMS])
        head_i = sb("head_i", [P, HEAD], I32)
        row_id = sb("row_id", [P, BT, FIELDS])
        not_index = sb("not_index", [P, 2, BT], U32)
        pair_index = sb("pair_index", [P, PAIR_ELEMENTS, QUARTERS, BT], U32)
        rest_index = sb("rest_index", [P, FIELDS, BT], U32)
        is_not = sb("is_not", [P, 3, PAIR_ELEMENTS])
        source_i = sb("source_i", [P, PAIR_ELEMENTS * KT], I32)
        rest = sb("rest", [P, 3, FIELDS])
        sc = sb("sc", [P, 8])
        b_sum = sb("b_sum", [P, KT])
        y = sb("y", [P, BT])

        gemm = ctx.enter_context(nc.psum_tensor("gemm", [P, 4, B], F32))
        flip = ctx.enter_context(nc.psum_tensor("flip", [P, 4, B], F32))

        not_rows_1 = nt[:, 0:8, :].rearrange("p t b -> p (t b)").rearrange("p (a h) -> p a h", a=BT)
        rest_rows = nt[:, 8:16, :].rearrange("p t b -> p (t b)").rearrange("p (a h) -> p a h", a=BT)
        neg = nt[:, 8, 0:BT * FIELDS].rearrange("p (t f) -> p t f", t=BT)
        elem_row = nt[:, 8, 64:64 + PICKED * BT].rearrange("p (s t) -> p s t", s=PICKED)
        pick = nt[:, 9, 0:PICKED * FIELDS].rearrange("p (s f) -> p s f", s=PICKED)
        source = nt[:, 9, 128:128 + PAIR_ELEMENTS * KT].rearrange("p (e k) -> p e k", k=KT)
        work = nt[:, 10, 0:PICKED * BT * FIELDS]
        head_f = nt[:, 11, 0:HEAD]
        ids = head_f[:, 0:HEAD_IDS].rearrange("p (t f) -> p t f", t=BT)
        fld = head_f[:, HEAD_IDS:HEAD_IDS + PICKED]
        con = head_f[:, HEAD_IDS + PICKED:HEAD]
        fld_neg = nt[:, 12, 0:PICKED]
        dense_raw = nt[0:DENSE_ROWS, 16, :]
        w_dense_raw = nt[0:DENSE_ROWS, 17, :]

        def first_tile(t):
            return gemm[:, t, :] if t < 4 else flip[:, t % 4, :]

        def one(tiles, k):
            return tiles[:, bass.ds(k, 1), :].rearrange("p o b -> p (o b)")

        row_quarters = tables.rearrange("r (q w) -> (r q) w", q=QUARTERS)

        head_in = sem("head_in")
        params_in = sem("params_in")
        ident_done = sem("ident_done")
        index_ops = sem("index_ops")
        not_index_done = sem("not_index_done")
        index_done = sem("index_done")
        rows_in = [sem(f"rows_in{s}") for s in range(4)]
        not_rows_in = sem("not_rows_in")
        flipped = sem("flipped")
        tile_hi = sem("tile_hi")
        staged = sem("staged")
        x_ready = sem("x_ready")
        x_used = sem("x_used")
        w_in = [sem(f"w_in{s}") for s in range(2)]
        w_hi_done = sem("w_hi_done")
        w_ready = sem("w_ready")
        w_begun = sem("w_begun")
        summed = sem("summed")
        activated = sem("activated")
        hi_done = sem("hi_done")
        evacuated = sem("evacuated")
        chain = sem("chain")
        rest_added = sem("rest_added")
        rest_flipped = sem("rest_flipped")
        dense_clear = sem("dense_clear")
        dense_in = sem("dense_in")
        dense_hi = sem("dense_hi")
        dense_ready = sem("dense_ready")
        y_done = sem("y_done")
        y_out = sem("y_out")
        stored = sem("stored")

        block = ctx.enter_context(nc.Block())

        def after_and_a(s):
            return 16 + (4 * 16 * BT if s < 2 else 0)

        def rows_first_pair(q):
            return 16 + 16 * BT * (q + 1)

        def rows_pair(stage, unit):
            return after_and_a(unit % 4) + 16 * BT * (2 * (stage - 1) + unit // 4 + 1)

        def rows_rest(field, bt):
            return after_and_a(bt) + 16 * BT * 4 + 16 * (field + 1)

        @block.sync
        def _(sp):
            sp.dma_start(head_i[:], head).then_inc(head_in, 16)
            for c in range(2):
                sp.dma_start(w_raw[:, c, :], weights[c]).then_inc(w_in[c], 16)

            def load(c, source_chunk, slot):
                sp.wait_ge(w_ready, c - 1)
                sp.dma_start(w_raw[:, slot, :], weights[bass.ds(source_chunk, 1)].rearrange("o p n -> (o p) n")
                             ).then_inc(w_in[slot], 16)

            sp.wait_ge(not_rows_in, 16 * BT)
            with sp.Fori(0, (AND_B - 2) // 2) as i:
                for s in range(2):
                    load(2 * i + 2 + s, 2 * i + 2 + s, s)
            with sp.Fori(0, (TOPB - AND_B) // 2) as i:
                for s in range(2):
                    load(2 * i + AND_B + s, 2 * i + AND_A + s, s)
            load(TOPB, TOPB - AND_AGAIN, TOPB % 2)
            sp.wait_ge(y_out, 1)
            sp.dma_start(out.rearrange("(p t) o -> p (t o)", p=P), y[:]).then_inc(stored, 16)
            sp.wait_ge(stored, 16)

        @block.gpsimd
        def _(pool):
            nc.gpsimd.memset(ident[:], 0.0).then_inc(ident_done, 1)
            pool.wait_ge(ident_done, 1)
            nc.gpsimd.affine_select(out=ident[:], in_=ident[:], compare_op=ALU.not_equal, fill=1.0, base=0,
                                    pattern=[[-1, P]], channel_multiplier=1).then_inc(ident_done, 1)

            def gather_rows(dst, index, done):
                nc.gpsimd.indirect_dma_start(
                    out=dst, out_offset=None, in_=tables,
                    in_offset=bass.IndirectOffsetOnAxis(ap=index, axis=0),
                    bounds_check=ROWS - 1, oob_is_err=False).then_inc(done, 16)

            def gather_quarter(slot, element, q):
                dst = rows[:, slot, :].rearrange("p (t w) -> p t w", t=BT)
                for bt in range(BT):
                    nc.gpsimd.indirect_dma_start(
                        out=dst[:, bt, :], out_offset=None, in_=row_quarters,
                        in_offset=bass.IndirectOffsetOnAxis(ap=pair_index[:, element, q, bt:bt + 1], axis=0),
                        bounds_check=ROWS * QUARTERS - 1, oob_is_err=False).then_inc(rows_in[slot], 16)

            pool.wait_ge(not_index_done, 1)
            for bt in range(BT):
                gather_rows(rows[:, bt, :], not_index[:, 0, bt:bt + 1], rows_in[bt])
            for bt in range(BT):
                gather_rows(not_rows_1[:, bt, :], not_index[:, 1, bt:bt + 1], not_rows_in)
            pool.wait_ge(index_done, 1)
            for q in range(QUARTERS):
                for e in range(2):
                    pool.wait_ge(flipped, KT if q == 0 else T_AND_A + 2 * (2 * q - 1) + e + 1)
                    gather_quarter(e, e, q)
            for stage, t0 in ((1, T_AND_B), (2, T_OR)):
                for unit in range(8):
                    q = unit % 4
                    if unit >= 4:
                        pool.wait_ge(flipped, t0 + 2 * q + 2)
                    elif stage == 1:
                        pool.wait_ge(flipped, T_AND_A + 15 + unit if unit < 2 else KT)
                    else:
                        pool.wait_ge(flipped, T_AND_B + 8 + 2 * q + 2)
                    gather_quarter(q, 2 * stage + unit // 4, q)
            for f in range(FIELDS):
                for bt in range(BT):
                    if f == 0:
                        pool.wait_ge(flipped, T_OR + 8 + 2 * bt + 2)
                    else:
                        pool.wait_ge(rest_added, (f - 1) * BT + bt + 1)
                    gather_rows(rows[:, bt, :], rest_index[:, f, bt:bt + 1], rows_in[bt])

        @block.scalar
        def _(act):
            act.dma_start(par[:], params).then_inc(params_in, 16)

            def weight_hi(c, slot, first=False):
                act.wait_ge(w_in[slot], 16 * (c // 2) + 16 if isinstance(c, int) else (c - slot) * 8 + 16)
                if not first:
                    act.wait_ge(w_begun, c)
                nc.scalar.activation(w_hi[:, slot, :], w_raw[:, slot, :], ACT.Copy).then_inc(w_hi_done, 1)

            def through(group, bank, func, bias_col, dst=None, hi=None):
                if group is not None:
                    act.wait_ge(summed, group + 1)
                g = gemm[:, bank, :]
                bias = par[:, bias_col:bias_col + 1] if isinstance(bias_col, int) else par[:, bass.ds(bias_col, 1)]
                if hi is not None:
                    nc.scalar.activation(hi, g, func, bias=bias)
                nc.scalar.activation(g if dst is None else dst, g, func, bias=bias).then_inc(activated, 1)

            def stage_tile(t):
                act.wait_ge(flipped, t + 1)
                if t >= T_AND_A + 2:
                    act.wait_ge(x_ready, t - 1)
                nc.scalar.activation(nt[:, 16 + t % 2, :], flip[:, t % 4, :], ACT.Copy).then_inc(staged, 1)

            weight_hi(0, 0, first=True)
            weight_hi(1, 1, first=True)
            for t in range(T_AND_A):
                act.wait_ge(flipped, t + 1)
                nc.scalar.activation(x[:, t // KT, 0, t % KT, :], first_tile(t), ACT.Copy).then_inc(tile_hi, 1)
            act.wait_ge(params_in, 16)
            with act.Fori(0, KT // 2) as i:
                for s in range(2):
                    weight_hi(2 * i + 2 + s, s)
                    act.wait_ge(summed, 4 * i + (2 * s + 2))
                    for f in range(2):
                        through(None, 2 * s + f, ACT.Relu, 2 * i + (C_BN1 + s), hi=one(hid[:, f, 0], 2 * i + s))
            for m in range(KT):
                weight_hi(NOT2 + m + 2, m % 2)
                for f in range(2):
                    through(G_NOT2 + 2 * m + f, 2 * (m % 2) + f, ACT.Tanh, C_BN2 + m, nt[:, KT * f + m, :])
                for e in range(2):
                    stage_tile(T_AND_A + 2 * m + e)
            for c0, g0, bias, nxt, hi in ((AND_A, G_AND_A, C_BA1, T_AND_B, hid[:, 0, 0]),
                                          (AND_B, G_AND_B, C_BA1, T_OR, None),
                                          (OR, G_OR, C_BO1, None, hid[:, 1, 0])):
                with act.Fori(0, 3) as j:
                    for c in range(4):
                        weight_hi(4 * j + (c0 + 2 + c), c % 2)
                    for i in range(2):
                        through(2 * j + (g0 + i), 2 * (j % 2) + i, ACT.Relu, 2 * j + (bias + i),
                                hi=None if hi is None else one(hi, 2 * j + i))
                if nxt is None:
                    act.wait_ge(dense_clear, 1)
                    for r in range(0, DENSE_ROWS, 32):
                        act.dma_start(dense_raw[r:r + DENSE, :], dense_t).then_inc(dense_in, 16)
                        act.dma_start(w_dense_raw[r:r + DENSE, :], w_dense).then_inc(dense_in, 16)
                for c in range(4):
                    if nxt is not None:
                        for k in range(4):
                            stage_tile(nxt + 4 * c + k)
                    weight_hi(c0 + 14 + c, c % 2)
                for i in range(2):
                    through(g0 + 6 + i, 2 + i, ACT.Relu, bias + 6 + i, hi=None if hi is None else hi[:, 6 + i, :])
            act.wait_ge(dense_in, 6 * 16)
            act.wait_ge(summed, G_SUM)
            nc.scalar.activation(x[0:DENSE_ROWS, 1, 0, 4, :], dense_raw, ACT.Copy).then_inc(dense_hi, 1)
            nc.scalar.activation(x[0:DENSE_ROWS, 1, 0, 5, :], w_dense_raw, ACT.Copy).then_inc(dense_hi, 1)
            for c in range(SUM + 2, CHUNKS):
                weight_hi(c, c % 2)
            for n in range(4):
                through(G_TOPA + n, n, ACT.Relu, C_BT1 + n, hi=x[:, 1, 0, n, :])
            for n in range(2):
                through(G_TOPB + n, n, ACT.Relu, C_BT2 + n, nt[:, n, :])

        @block.vector
        def _(dve):
            small = [0]

            def step(instruction):
                small[0] += 1
                instruction.then_inc(index_ops, 1)
                dve.wait_ge(index_ops, small[0])

            voc, last, base, iota = (con[:, c:c + FIELDS] for c in (K_VOC, K_LAST, K_BASE, K_IOTA))
            by_bt = [v.unsqueeze(1).to_broadcast([P, BT, FIELDS]) for v in (voc, last, base)]

            dve.wait_ge(head_in, 16)
            step(nc.vector.tensor_copy(head_f, head_i[:]))
            nc.vector.scalar_tensor_tensor(out=neg, in0=ids, scalar=0.0, in1=by_bt[0], op0=ALU.is_lt, op1=ALU.mult)
            step(nc.vector.tensor_scalar(fld_neg, fld, 0.0, float(FIELDS), ALU.is_lt, ALU.mult))
            nc.vector.tensor_tensor(row_id[:], ids, neg, ALU.add)
            step(nc.vector.tensor_tensor(fld, fld, fld_neg, ALU.add))
            nc.vector.tensor_tensor(pick, fld.unsqueeze(2).to_broadcast([P, PICKED, FIELDS]),
                                    iota.unsqueeze(1).to_broadcast([P, PICKED, FIELDS]), ALU.is_equal)
            step(nc.vector.scalar_tensor_tensor(out=row_id[:], in0=row_id[:], scalar=0.0, in1=by_bt[1],
                                                op0=ALU.max, op1=ALU.min))
            step(nc.vector.tensor_tensor(row_id[:], row_id[:], by_bt[2], ALU.add))
            by_slot = work.rearrange("p (s t f) -> p s t f", s=PICKED, t=BT)
            shape = [P, PICKED, BT, FIELDS]
            step(nc.vector.tensor_tensor(by_slot, pick.unsqueeze(2).to_broadcast(shape),
                                         row_id[:].unsqueeze(1).to_broadcast(shape), ALU.mult))
            step(nc.vector.tensor_reduce(elem_row, by_slot, AX.X, ALU.add))
            nc.vector.tensor_copy(not_index[:], elem_row[:, 0:2, :]).then_inc(not_index_done, 1)

            for j in range(2):
                nc.vector.tensor_scalar(is_not[:, j, :], fld[:, 2:PICKED], fld[:, j:j + 1], None, ALU.is_equal)
            step(nc.vector.tensor_scalar(sc[:, 3:4], fld[:, 0:1], fld[:, 1:2], None, ALU.is_equal))
            step(nc.vector.tensor_tensor(is_not[:, 2, :], is_not[:, 0, :], is_not[:, 1, :], ALU.max))
            step(nc.vector.tensor_tensor(is_not[:, 1, :], is_not[:, 2, :], is_not[:, 0, :], ALU.subtract))
            step(nc.vector.tensor_scalar(elem_row[:, 2:PICKED, :], elem_row[:, 2:PICKED, :], float(QUARTERS), None,
                                         ALU.mult))
            either = is_not[:, 2, :].unsqueeze(2).to_broadcast([P, PAIR_ELEMENTS, BT])
            step(nc.vector.scalar_tensor_tensor(out=elem_row[:, 2:PICKED, :], in0=either, scalar=BIG,
                                                in1=elem_row[:, 2:PICKED, :], op0=ALU.mult, op1=ALU.add))
            for q in range(QUARTERS):
                nc.vector.tensor_scalar(pair_index[:, :, q, :], elem_row[:, 2:PICKED, :], float(q), None, ALU.add)
            shape = [P, PAIR_ELEMENTS, KT]
            src = source
            tmp = work[:, 0:PAIR_ELEMENTS * KT].rearrange("p (e k) -> p e k", k=KT)
            tile_no = con[:, K_TILE:K_TILE + 48].rearrange("p (e k) -> p e k", k=KT)
            place = con[:, K_STAGE:K_STAGE + 48].rearrange("p (e k) -> p e k", k=KT)
            step(nc.vector.tensor_tensor(src, tile_no, place, ALU.subtract))
            step(nc.vector.tensor_tensor(src, src, is_not[:, 2, :].unsqueeze(2).to_broadcast(shape), ALU.mult))
            step(nc.vector.tensor_tensor(src, src, place, ALU.add))
            step(nc.vector.scalar_tensor_tensor(out=tmp, in0=is_not[:, 1, :].unsqueeze(2).to_broadcast(shape),
                                                scalar=float(KT), in1=src, op0=ALU.mult, op1=ALU.add))
            step(nc.vector.tensor_scalar(source_i[:].rearrange("p (e k) -> p e k", k=KT), tmp, float(B), None,
                                         ALU.mult))
            step(nc.vector.tensor_reduce(rest[:, 0, :], pick[:, 2:PICKED, :].rearrange("p s f -> p f s"), AX.X,
                                         ALU.max))
            step(nc.vector.tensor_scalar(rest[:, 0, :], rest[:, 0, :], -1.0, 1.0, ALU.mult, ALU.add))
            step(nc.vector.tensor_tensor(rest[:, 1, :], pick[:, 0, :], pick[:, 1, :], ALU.max))
            step(nc.vector.tensor_tensor(rest[:, 1, :], rest[:, 0, :], rest[:, 1, :], ALU.mult))
            step(nc.vector.tensor_tensor(rest[:, 2, :], rest[:, 0, :], rest[:, 1, :], ALU.subtract))
            both = work[:, 0:2 * FIELDS].rearrange("p (j f) -> p j f", j=2)
            step(nc.vector.tensor_tensor(both, pick[:, 0:2, :],
                                         rest[:, 0, :].unsqueeze(1).to_broadcast([P, 2, FIELDS]), ALU.mult))
            step(nc.vector.tensor_reduce(sc[:, 0:2], both, AX.X, ALU.add))
            step(nc.vector.tensor_reduce(sc[:, 2:3], rest[:, 0, :], AX.X, ALU.add))
            step(nc.vector.tensor_scalar(sc[:, 2:3], sc[:, 2:3], 3.0, None, ALU.add))
            step(nc.vector.reciprocal(sc[:, 2:3], sc[:, 2:3]))
            step(nc.vector.tensor_scalar(sc[:, 3:4], sc[:, 3:4], -1.0, 1.0, ALU.mult, ALU.add))
            step(nc.vector.tensor_tensor(sc[:, 1:2], sc[:, 1:2], sc[:, 3:4], ALU.mult))
            step(nc.vector.tensor_scalar(rest[:, 1, :], rest[:, 2, :], -BIG, BIG, ALU.mult, ALU.add))
            step(nc.vector.tensor_tensor(rest_index[:].rearrange("p f t -> p t f"), row_id[:],
                                         rest[:, 1, :].unsqueeze(1).to_broadcast([P, BT, FIELDS]), ALU.add))
            dve.wait_ge(params_in, 16)
            nc.vector.scalar_tensor_tensor(out=b_sum[:], in0=par[:, C_BA2:C_BA2 + KT], scalar=2.0,
                                           in1=par[:, C_BO2:C_BO2 + KT], op0=ALU.mult, op1=ALU.add
                                           ).then_inc(index_done, 1)

            def weight_lo(c, slot):
                dve.wait_ge(w_hi_done, c + 1)
                nc.vector.tensor_tensor(w_lo[:, slot, :], w_raw[:, slot, :], w_hi[:, slot, :].bitcast(F32),
                                        ALU.subtract).then_inc(w_ready, 1)

            def split(src, hi, lo, n, done):
                nc.vector.tensor_copy(hi, src).then_inc(hi_done, 1)
                dve.wait_ge(hi_done, n + 1)
                nc.vector.tensor_tensor(lo, src, hi.bitcast(F32), ALU.subtract).then_inc(done, 1)

            def lo_part(src, hi, lo):
                nc.vector.tensor_tensor(lo, src, hi.bitcast(F32), ALU.subtract).then_inc(evacuated, 1)

            weight_lo(0, 0)
            weight_lo(1, 1)
            for t in range(T_AND_A):
                dve.wait_ge(tile_hi, t + 1)
                nc.vector.tensor_tensor(x[:, t // KT, 1, t % KT, :], first_tile(t),
                                        x[:, t // KT, 0, t % KT, :].bitcast(F32), ALU.subtract).then_inc(x_ready, 1)
            with dve.Fori(0, KT // 2) as i:
                for s in range(2):
                    weight_lo(2 * i + 2 + s, s)
                    for f in range(2):
                        n = 4 * i + 2 * s + f
                        dve.wait_ge(activated, n + 1)
                        lo_part(gemm[:, 2 * s + f, :], one(hid[:, f, 0], 2 * i + s), one(hid[:, f, 1], 2 * i + s))
            his = [0]
            chained = [0]

            def pair_tile(t, stage, e, k):
                place = dve.value_load(source_i[0:1, (2 * stage + e) * KT + k:(2 * stage + e) * KT + k + 1],
                                       min_val=0, max_val=17 * B)
                src = nt[:].rearrange("p t b -> p (t b)")[:, bass.ds(place, B)]
                dve.wait_ge(staged, t - T_AND_A + 1)
                if stage == 0:
                    dve.wait_ge(activated, G_NOT2 + 2 * k + 2)
                    dve.wait_ge(w_begun, NOT2 + 1)
                else:
                    dve.wait_ge(x_used, 16 * (stage - 1) + 8 * e + k + 1)
                split(src, x[:, e, 0, k, :], x[:, e, 1, k, :], his[0], x_ready)
                his[0] += 1

            for m in range(KT):
                weight_lo(NOT2 + m + 2, m % 2)
                for e in range(2):
                    pair_tile(T_AND_A + 2 * m + e, 0, e, m)

            def hidden_out(e, m, g):
                dve.wait_ge(activated, g + 1)
                lo_part(gemm[:, m % 4, :], hid[:, e, 0, m, :], hid[:, e, 1, m, :])

            def add_hidden_out(m, bank, g):
                dve.wait_ge(activated, g + 1)
                for part in range(2):
                    nc.vector.tensor_tensor(gemm[:, bank, :], gemm[:, bank, :], hid[:, 0, part, m, :].bitcast(F32),
                                            ALU.add).then_inc(chain, 1)
                    chained[0] += 1
                    dve.wait_ge(chain, chained[0])
                split(gemm[:, bank, :], hid[:, 0, 0, m, :], hid[:, 0, 1, m, :], his[0], evacuated)
                his[0] += 1

            def pair_stage(c0, evacuate, extras):
                for n in range(16):
                    extras(n)
                    weight_lo(c0 + 2 + n, n % 2)
                    if n % 4 == 3:
                        for i in range(2):
                            evacuate(2 * (n // 4) + i)

            def first_out(m):
                hidden_out(0, m, G_AND_A + m)

            def second_out(m):
                add_hidden_out(m, m % 4, G_AND_B + m)

            def or_out(m):
                hidden_out(1, m, G_OR + m)

            def next_tiles(stage, t0):
                def extras(n):
                    if n >= 12:
                        for s in range(4 * (n - 12), 4 * (n - 12) + 4):
                            pair_tile(t0 + s, stage, s // KT, s % KT)
                return extras

            def chained_step(instruction):
                chained[0] += 1
                instruction.then_inc(chain, 1)
                dve.wait_ge(chain, chained[0])

            def rest_sums(n):
                if n == 4:
                    nc.vector.memset(nt[0:DENSE_ROWS, 16:18, :], 0.0).then_inc(dense_clear, 1)
                if n < 4:
                    for k in ((), (0, 1, 2), (3, 4, 5), (6, 7))[n]:
                        chained_step(nc.vector.tensor_scalar(nt[:, k, :], nt[:, k, :], sc[:, 0:1], None, ALU.mult))
                        chained_step(nc.vector.scalar_tensor_tensor(
                            out=nt[:, k, :], in0=nt[:, KT + k, :], scalar=sc[:, 1:2], in1=nt[:, k, :],
                            op0=ALU.mult, op1=ALU.add))
                    return
                for r in range(2 * (n - 4), 2 * (n - 4) + 2):
                    f, bt = r // BT, r % BT
                    dve.wait_ge(rows_in[bt], rows_rest(f, bt))
                    weight = rest[:, 2, f:f + 1]
                    if f == 0:
                        nc.vector.tensor_scalar(rest_rows[:, bt, :], rows[:, bt, :], weight, None, ALU.mult
                                                ).then_inc(rest_added, 1)
                    else:
                        dve.wait_ge(rest_added, r - BT + 1)
                        nc.vector.scalar_tensor_tensor(out=rest_rows[:, bt, :], in0=rows[:, bt, :], scalar=weight,
                                                       in1=rest_rows[:, bt, :], op0=ALU.mult, op1=ALU.add
                                                       ).then_inc(rest_added, 1)

            def rest_tile(m):
                dve.wait_ge(flipped, T_REST + m + 1)
                nc.vector.scalar_tensor_tensor(out=nt[:, m, :], in0=flip[:, m % 4, :], scalar=b_sum[:, m:m + 1],
                                               in1=nt[:, m, :], op0=ALU.add, op1=ALU.add).then_inc(rest_flipped, 1)

            def field_sum(m):
                bank = gemm[:, m % 4, :]
                dve.wait_ge(summed, G_SUM + m + 1)
                dve.wait_ge(rest_flipped, m + 1)
                chained_step(nc.vector.tensor_tensor(bank, bank, nt[:, m, :], ALU.add))
                nc.vector.tensor_scalar(x[:, 0, 0, m, :], bank, sc[:, 2:3], None, ALU.mult).then_inc(hi_done, 1)
                his[0] += 1
                dve.wait_ge(hi_done, his[0])
                nc.vector.scalar_tensor_tensor(out=x[:, 0, 1, m, :], in0=bank, scalar=sc[:, 2:3],
                                               in1=x[:, 0, 0, m, :].bitcast(F32), op0=ALU.mult, op1=ALU.subtract
                                               ).then_inc(evacuated, 1)

            pair_stage(AND_A, first_out, next_tiles(1, T_AND_B))
            pair_stage(AND_B, second_out, next_tiles(2, T_OR))
            pair_stage(OR, or_out, rest_sums)
            dve.wait_ge(dense_hi, 2)
            for n, raw, r in ((4, dense_raw, 32), (5, w_dense_raw, 64)):
                own = x[r:r + DENSE, 1, 0, n, :]
                nc.vector.tensor_tensor(own, raw[r:r + DENSE, :], own.bitcast(F32), ALU.subtract
                                        ).then_inc(dense_ready, 1)
            for n in range(16):
                if n < 4:
                    rest_sums(16 + n)
                weight_lo(SUM + 2 + n, n % 2)
                for m in {4: range(4), 8: (4, 5), 12: (6, 7)}.get(n, ()):
                    rest_tile(m)
                for m in {4: (0, 1), 7: (2, 3), 11: (4, 5), 15: (6, 7)}.get(n, ()):
                    field_sum(m)
            for c in range(TOPA + 2, CHUNKS):
                weight_lo(c, c % 2)
            for n in range(4):
                dve.wait_ge(activated, G_SUM + n + 1)
                lo_part(gemm[:, n, :], x[:, 1, 0, n, :], x[:, 1, 1, n, :])
            dve.wait_ge(y_done, 1)
            nc.vector.tensor_copy(y[:], flip[:, 0, 0:BT]).then_inc(y_out, 1)

        @block.tensor
        def _(pe):
            def product(dst, slot, wcol, moving, k, start, stop, begins_chunk=False):
                wh, wl = w_hi[:, slot, wcol:wcol + P], w_lo[:, slot, wcol:wcol + P]
                first = nc.tensor.matmul(dst, wh, moving[:, 0, k, :], start=start, stop=False)
                if begins_chunk:
                    first.then_inc(w_begun, 1)
                nc.tensor.matmul(dst, wh, moving[:, 1, k, :], start=False, stop=False)
                return nc.tensor.matmul(dst, wl, moving[:, 0, k, :], start=False, stop=stop)

            def flip_tile(t, src, past=None):
                for bt in range(BT):
                    last = nc.tensor.transpose(flip[:, t % 4, bt * P:(bt + 1) * P], src(bt), ident[:])
                    if bt == 0 and past is not None:
                        last.then_inc(past, 1)
                last.then_inc(flipped, 1)

            def flip_second(k):
                if k == 0:
                    pe.wait_ge(not_rows_in, 16 * BT)
                pe.wait_ge(x_ready, KT + k - 3)
                flip_tile(KT + k, lambda bt: not_rows_1[:, bt, k * P:(k + 1) * P])

            def quarter_tile(t, slot, k, past=None):
                part = rows[:, slot, :].rearrange("p (t w) -> p t w", t=BT)
                flip_tile(t, lambda bt: part[:, bt, (k % 2) * P:(k % 2) * P + P], past)

            def nothing(*_):
                pass

            def field_group(slot, f, moving, waits=nothing, after=nothing):
                for k in range(KT):
                    waits(k)
                    last = product(gemm[:, 2 * slot + f, :], slot, k * P, moving[:, f], k, k == 0, k == KT - 1,
                                   begins_chunk=(f == 0 and k == 0))
                    if k == KT - 1:
                        last.then_inc(summed, 1)
                    after(k)

            pe.wait_ge(ident_done, 2)
            for n in range(WARM):
                nc.tensor.matmul(gemm[:, 0, 0:P], ident[:], ident[:], start=True, stop=True)
            for bt in range(BT):
                pe.wait_ge(rows_in[bt], 16)
                for k in range(KT):
                    last = nc.tensor.transpose(first_tile(k)[:, bt * P:(bt + 1) * P], rows[:, bt, k * P:(k + 1) * P],
                                               ident[:])
                    if bt == BT - 1:
                        last.then_inc(flipped, 1)

            pe.wait_ge(w_ready, 1)
            field_group(0, 0, x, lambda k: pe.wait_ge(x_ready, k + 1))
            for k in range(4):
                flip_second(k)
            field_group(0, 1, x, lambda k: pe.wait_ge(x_ready, KT + k + 1),
                        lambda k: flip_second(k + 4) if k < 4 else None)
            pe.wait_ge(w_ready, 2)
            field_group(1, 0, x)
            field_group(1, 1, x)
            with pe.Fori(1, KT // 2) as i:
                for s in range(2):
                    pe.wait_ge(w_ready, 2 * i + (s + 1))
                    for f in range(2):
                        pe.wait_ge(evacuated, 4 * i + (2 * s + f - 3))
                        field_group(s, f, x)

            def second_layer(m, s, q, first):
                pe.wait_ge(w_ready, m + (NOT2 + 1))
                for f in range(2):
                    if first:
                        pe.wait_ge(evacuated, G_NOT2 + 2 * s + f - 3)
                    else:
                        pe.wait_ge(activated, 2 * m + (G_NOT2 + f - 3))
                    waits = (lambda k: pe.wait_ge(evacuated, 2 * k + f + 1)) if first and s == 0 else nothing
                    field_group(s, f, hid, waits)
                for e in range(2):
                    pe.wait_ge(rows_in[e], q * (16 * BT) + rows_first_pair(0))
                    if first:
                        pe.wait_ge(x_ready, T_AND_A)
                    else:
                        pe.wait_ge(staged, 2 * m + (e - 3))
                    quarter_tile(2 * s + e, e, s)

            for s in range(2):
                second_layer(s, s, 0, True)
            with pe.Fori(1, KT // 2) as i:
                for s in range(2):
                    second_layer(2 * i + s, s, i, False)

            def two_tiles(c0, moving, j, bank, bank_wait, tile_wait, after, tiles=16):
                for s in range(tiles):
                    slot, kk = (s // 4) % 2, s % 4
                    if kk == 0:
                        pe.wait_ge(w_ready, 4 * j + (c0 + s // 4 + 1))
                    tile_wait(s)
                    for i in range(2):
                        if s == 0:
                            bank_wait(i)
                        wcol = kk * 2 * P + i * P
                        dst = gemm[:, bank + i, :] if isinstance(bank, int) else \
                            gemm[:, bass.ds(bank + i, 1), :].rearrange("p o b -> p (o b)")
                        e, k = s // KT, s % KT
                        last = product(dst, slot, wcol, moving[:, e], k, s == 0, s == tiles - 1,
                                       begins_chunk=(kk == 0 and i == 0))
                        if s == tiles - 1:
                            last.then_inc(summed, 1)
                    after(s)

            def stage(c0, moving, ready, bank_wait, after_last):
                with pe.Fori(0, 3) as j:
                    two_tiles(c0, moving, j, 2 * (j % 2), lambda i: bank_wait(j, i), ready, nothing)
                two_tiles(c0, moving, 3, 2, lambda i: bank_wait(3, i), nothing, after_last)

            def flip_next(t0, pair):
                def after(s):
                    pe.wait_ge(rows_in[(s // 2) % 4], rows_pair(pair, s // 2))
                    pe.wait_ge(staged, t0 + s - 3 - T_AND_A)
                    quarter_tile(t0 + s, (s // 2) % 4, s, x_used)
                return after

            def evac_wait(g0):
                return lambda j, i: pe.wait_ge(evacuated, 2 * j + (g0 - 16 + i - 3))

            def and_a_wait(j, i):
                pe.wait_ge(activated, 2 * j + (G_AND_A + i - 3))
                pe.wait_ge(evacuated, 2 * j + (G_AND_A - 16 + i - 3))

            stage(AND_A, x, lambda s: pe.wait_ge(x_ready, T_AND_A + 2 * (s % KT) + s // KT + 1),
                  and_a_wait, flip_next(T_AND_B, 1))
            stage(AND_B, x, lambda s: pe.wait_ge(x_ready, T_AND_B + s + 1), evac_wait(G_AND_B), flip_next(T_OR, 2))
            stage(OR, x, lambda s: pe.wait_ge(x_ready, T_OR + s + 1), evac_wait(G_OR), nothing)

            def hidden_ready(s):
                pe.wait_ge(evacuated, (G_AND_B if s < KT else G_OR) - 16 + s % KT + 1)

            def flip_rest(m):
                pe.wait_ge(rest_added, FIELDS * BT)
                if m < 4:
                    pe.wait_ge(staged, T_REST - T_AND_A)
                else:
                    pe.wait_ge(rest_flipped, m - 3)
                flip_tile(T_REST + m, lambda bt: rest_rows[:, bt, m * P:(m + 1) * P])

            for j in range(4):
                def after(s, j=j):
                    if s == 3:
                        for m in ((), range(4), (4, 5), (6, 7))[j]:
                            flip_rest(m)
                two_tiles(SUM, hid, j, 2 * (j % 2), lambda i, j=j: evac_wait(G_SUM)(j, i),
                          hidden_ready if j == 0 else nothing, after)

            for j in range(2):
                for s in range(KT):
                    slot, kk = (s // 4) % 2, s % 4
                    if kk == 0:
                        pe.wait_ge(w_ready, TOPA + 2 * j + s // 4 + 1)
                    if j == 0:
                        pe.wait_ge(evacuated, G_SUM - 16 + s + 1)
                    for i in range(2):
                        if s == 0:
                            pe.wait_ge(evacuated, G_TOPA - 16 + 2 * j + i - 3)
                        last = product(gemm[:, 2 * j + i, :], slot, kk * 2 * P + i * P, x[:, 0], s, s == 0, False,
                                       begins_chunk=(kk == 0 and i == 0))
                if j == 0:
                    pe.wait_ge(dense_ready, 2)
                for i in range(2):
                    m = (2 * j + i) * P
                    dst = gemm[:, 2 * j + i, :]
                    nc.tensor.matmul(dst, x[0:DENSE_ROWS, 1, 0, 5, m:m + P], x[0:DENSE_ROWS, 1, 0, 4, :],
                                     start=False, stop=True).then_inc(summed, 1)
            pe.wait_ge(w_ready, TOPB + 1)
            for s in range(TOP1 // P):
                pe.wait_ge(evacuated, G_TOPA - 16 + s + 1)
                for i in range(2):
                    if s == 0 and i == 1:
                        pe.wait_ge(evacuated, G_TOPA - 16 + 2)
                    last = product(gemm[:, i, :], TOPB % 2, s * 2 * P + i * P, x[:, 1], s, s == 0, s == 3)
                    if s == 3:
                        last.then_inc(summed, 1)
            for i in range(2):
                pe.wait_ge(activated, G_SUM + 4 + i + 1)
            for bt in range(BT):
                for k in range(2):
                    last = nc.tensor.matmul(flip[:, 0, bt:bt + 1], nt[:, k, bt * P:(bt + 1) * P],
                                            par[:, C_W3 + k:C_W3 + k + 1], start=(k == 0), stop=(k == 1))
            last.then_inc(y_done, 1)


def kernel(**inputs):
    import concourse.bacc as bacc
    from concourse.bass_utils import run_bass_kernel_spmd

    a = {k: np.asarray(v) for k, v in inputs.items()}
    g = {k[7:]: v for k, v in a.items() if k.startswith("L0_rec_")}

    def by_output_tile(w):
        return w.reshape(KT, P, KT, P).transpose(2, 1, 0, 3).reshape(-1, P, CHUNK)

    def by_output_pair(w):
        k, m = w.shape
        return w.reshape(k // 512, 4, P, m // 256, 256).transpose(3, 0, 2, 1, 4).reshape(-1, P, CHUNK)

    weights = np.concatenate([
        by_output_tile(g["Wn1"]), by_output_tile(g["Wn2"]), by_output_pair(g["Wa1"]), by_output_pair(g["Wo1"]),
        by_output_pair(np.concatenate([g["Wa2"], g["Wo2"]])), by_output_pair(a["W_top1"][:H]),
        by_output_pair(a["W_top2"])])
    params = np.concatenate([v.reshape(-1, P).T for v in (
        g["bn1"], g["bn2"], g["ba1"], g["ba2"], g["bo1"], g["bo2"], a["b_top1"], a["b_top2"], a["W_top3"])], axis=1)
    fields = np.concatenate([g["not_idx"].reshape(-1), g["and_pairs"].reshape(-1), g["or_pairs"].reshape(-1)])
    fixed = np.concatenate([fields, constants()])
    arrays = {
        "head": np.concatenate([a["ids"].reshape(P, HEAD_IDS), np.broadcast_to(fixed, (P, len(fixed)))], axis=1),
        "params": params, "tables": np.concatenate([a[f"tbl_{f}"] for f in range(FIELDS)]), "weights": weights,
        "dense_t": a["dense_ctx"].reshape(P, BT, DENSE).transpose(2, 1, 0).reshape(DENSE, B), "w_dense": a["W_top1"][H:],
    }
    arrays = {k: np.ascontiguousarray(v) for k, v in arrays.items()}
    nc = bacc.Bacc("TRN2", target_bir_lowering=False, num_devices=1)
    aps = {k: nc.dram_tensor(k, v.shape, mybir.dt.from_np(v.dtype), kind="ExternalInput").ap()
           for k, v in arrays.items()}
    aps["out"] = nc.dram_tensor("out", (B, 1), F32, kind="ExternalOutput").ap()
    build(nc, **aps)
    return run_bass_kernel_spmd(nc, [arrays], core_ids=[0]).results[0]["out"]
```
